# Optimizing a Trainium2 kernel written in Bass

```python
import numpy as np
import jax
import jax.numpy as jnp

def _softmax(x, axis=-1):
    return jax.nn.softmax(x, axis=axis)

def _gelu(x):
    return jax.nn.gelu(x, approximate=True)

def _silu(x):
    return jax.nn.silu(x)

def _sigmoid(x):
    return jax.nn.sigmoid(x)

def _layernorm(x, axis=-1, eps=1e-05):
    m = jnp.mean(x, axis=axis, keepdims=True)
    v = jnp.var(x, axis=axis, keepdims=True)
    return (x - m) / jnp.sqrt(v + eps)

def _scatter_add(tgt, idx, src, axis=0):
    return tgt.at[idx].add(src)

def _segment_sum(src, seg, n):
    return jax.ops.segment_sum(src, seg, n)
kernel_name = 'mk_adj_preln_d1_adj_r2_a1190a'

def setup_inputs(seed: int=0):
    np.random.seed(seed)
    _w = jnp.asarray

    def _rec_inputs():
        import jax
        import jax.numpy as jnp
        _gk = jax.random.key(seed)
        x = -0.0005207 + 1.001 * jax.random.normal(jax.random.fold_in(_gk, 1), (4096, 128), jnp.float32)
        _a = jax.random.bernoulli(jax.random.fold_in(_gk, 2), 0.00195312, (4096, 4096))
        _a = jnp.logical_or(_a, jnp.eye(4096, dtype=bool))
        _af = _a.astype(jnp.float32)
        _af = _af * jax.random.uniform(jax.random.fold_in(_gk, 3), (4096, 4096), jnp.float32, 0.05, 1)
        adj = _af
        return (x, adj)
    x, adj = _rec_inputs()

    def _L0_gnn_setup():
        import jax, jax.numpy as jnp
        import numpy as np
        D_IN = 128
        D_ATTN = 64
        STEPS = 2
        TOP_P = 0.9
        TAU = 1.0
        LN_EPS = 1e-05
        N_NODES = 4096

        def _top_p_attention(X, W1, W2, W3):
            q = X @ W1.T @ W2.T
            k = X @ W3.T
            logits = q @ k.T / TAU
            probs = jax.nn.softmax(logits, axis=-1)
            idx = jnp.argsort(-probs, axis=-1)
            sp = jnp.take_along_axis(probs, idx, axis=-1)
            cs = jnp.cumsum(sp, axis=-1)
            keep_sorted = cs - sp < TOP_P
            rows = jnp.arange(probs.shape[0])[:, None]
            mask = jnp.zeros(probs.shape, dtype=bool).at[rows, idx].set(keep_sorted)
            A = probs * mask
            return A / jnp.maximum(A.sum(-1, keepdims=True), 1e-12)
        key = jax.random.key(seed)
        ks = jax.random.split(key, 8)
        N, d, da, steps = (N_NODES, D_IN, D_ATTN, STEPS)
        X = jax.random.normal(ks[0], (N, d), dtype=jnp.float32)
        S = jax.random.uniform(ks[1], (N, N), dtype=jnp.float32)
        W1 = jax.random.normal(ks[2], (da, d), dtype=jnp.float32) / np.sqrt(d)
        W2 = jax.random.normal(ks[3], (da, da), dtype=jnp.float32) / np.sqrt(da)
        W3 = jax.random.normal(ks[4], (da, d), dtype=jnp.float32) / np.sqrt(d)
        U1 = jax.random.normal(ks[5], (steps, d, d), dtype=jnp.float32) / np.sqrt(d)
        U2 = jax.random.normal(ks[6], (steps, d, d), dtype=jnp.float32) / np.sqrt(d)
        ln_g = jnp.ones((d,), dtype=jnp.float32)
        ln_b = jnp.zeros((d,), dtype=jnp.float32)
        return {'X': X, 'S': S, 'W1': W1, 'W2': W2, 'W3': W3, 'U1': U1, 'U2': U2, 'ln_g': ln_g, 'ln_b': ln_b}
    _L0_gnn_all = _L0_gnn_setup()
    _L0_gnn_in = {k: v for k, v in _L0_gnn_all.items() if k in ('W1', 'W2', 'W3', 'U1', 'U2', 'ln_g', 'ln_b')}
    del _L0_gnn_all
    return {'x': x, 'adj': adj, 'L0_gnn_W1': _L0_gnn_in['W1'], 'L0_gnn_W2': _L0_gnn_in['W2'], 'L0_gnn_W3': _L0_gnn_in['W3'], 'L0_gnn_U1': _L0_gnn_in['U1'], 'L0_gnn_U2': _L0_gnn_in['U2'], 'L0_gnn_ln_g': _L0_gnn_in['ln_g'], 'L0_gnn_ln_b': _L0_gnn_in['ln_b']}

def reference(x, adj, L0_gnn_W1, L0_gnn_W2, L0_gnn_W3, L0_gnn_U1, L0_gnn_U2, L0_gnn_ln_g, L0_gnn_ln_b):
    import jax
    import jax.numpy as jnp

    def _L0_gnn_ref(X, S, W1, W2, W3, U1, U2, ln_g, ln_b):
        import jax, jax.numpy as jnp
        import numpy as np
        D_IN = 128
        D_ATTN = 64
        STEPS = 2
        TOP_P = 0.9
        TAU = 1.0
        LN_EPS = 1e-05
        N_NODES = 4096

        def _top_p_attention(X, W1, W2, W3):
            q = X @ W1.T @ W2.T
            k = X @ W3.T
            logits = q @ k.T / TAU
            probs = jax.nn.softmax(logits, axis=-1)
            idx = jnp.argsort(-probs, axis=-1)
            sp = jnp.take_along_axis(probs, idx, axis=-1)
            cs = jnp.cumsum(sp, axis=-1)
            keep_sorted = cs - sp < TOP_P
            rows = jnp.arange(probs.shape[0])[:, None]
            mask = jnp.zeros(probs.shape, dtype=bool).at[rows, idx].set(keep_sorted)
            A = probs * mask
            return A / jnp.maximum(A.sum(-1, keepdims=True), 1e-12)
        N = X.shape[0]
        R = S + jnp.eye(N, dtype=X.dtype)
        R = R / R.sum(-1, keepdims=True)
        Z = jnp.zeros_like(X)
        Xf = X
        Xa = X
        for n in range(STEPS):
            A = _top_p_attention(Xa, W1, W2, W3)
            Xf = R @ Xf
            Xa = A @ Xa
            Z = Z + Xf @ U1[n].T + Xa @ U2[n].T
        h = X + Z
        mu = h.mean(-1, keepdims=True)
        var = jnp.mean((h - mu) ** 2, axis=-1, keepdims=True)
        return (h - mu) / jnp.sqrt(var + LN_EPS) * ln_g + ln_b
    h = jnp.maximum(_layernorm(x, axis=-1), 0.0)
    x = x + _L0_gnn_ref(h, adj, L0_gnn_W1, L0_gnn_W2, L0_gnn_W3, L0_gnn_U1, L0_gnn_U2, L0_gnn_ln_g, L0_gnn_ln_b)
    return x

_drawn_inputs = setup_inputs


def setup_inputs(seed=0):
    import zlib

    import numpy as np

    out = dict(_drawn_inputs(seed))
    spreads = {'L0_gnn_ln_g': (1.0, 0.2), 'L0_gnn_ln_b': (0.0, 0.1)}
    factors = {}
    for name, (base, spread) in spreads.items():
        noise = np.random.default_rng([zlib.crc32(name.encode()), seed]).standard_normal(out[name].shape)
        drawn = base * np.exp(spread * noise) if base else spread * noise
        out[name] = jnp.asarray(drawn.astype(out[name].dtype))
    for name, factor in factors.items():
        out[name] = (out[name] * factor).astype(out[name].dtype)
    return out
```

```python
from contextlib import ExitStack

import concourse.bass as bass
from concourse import mybir

F32 = mybir.dt.float32
BF16 = mybir.dt.bfloat16
I32 = mybir.dt.int32
ALU = mybir.AluOpType
ACT = mybir.ActivationFunctionType
AX = mybir.AxisListType

P = 128
STEPS = 2
TOP_P = 0.9
LN_EPS = 1e-5
BANK = 512
BISECTIONS = 42


def program(nc, x, adj_t, w1, w2_t, w3_t, u1_t, u2_t, ln_g, ln_b, eye, out):
    N, D = x.shape
    DA = w1.shape[0]
    NT = N // P
    PAIRS = NT // 2
    CHUNK = 2 * BANK
    NC = N // CHUNK
    NB = N // BANK
    JC = 4
    AB = 4
    AC = NT // JC
    FILLS = NB + (PAIRS - 1) * (2 * NB + 2) + NB + 2

    xa_dram = nc.dram_tensor("xa_next", [N, D], F32, kind="Internal").ap()
    xf_dram = nc.dram_tensor("xf_next", [N, D], F32, kind="Internal").ap()
    z_dram = nc.dram_tensor("z_sum", [N, D], F32, kind="Internal").ap()

    def tiled(ap):
        return ap.rearrange("(t p) d -> p t d", p=P)

    with ExitStack() as ctx:
        def sb(name, shape, dt=F32):
            return ctx.enter_context(nc.sbuf_tensor(name, shape, dt))

        def sem(name):
            return ctx.enter_context(nc.semaphore(name))

        ps_logits = ctx.enter_context(nc.psum_tensor("ps_logits", [P, 2, CHUNK], F32))
        ps_turn = ctx.enter_context(nc.psum_tensor("ps_turn", [P, 2, BANK], F32))
        ps_att = ctx.enter_context(nc.psum_tensor("ps_att", [P, BANK], F32))
        ps_adj = ctx.enter_context(nc.psum_tensor("ps_adj", [P, BANK], F32))

        xa = sb("xa", [P, NT, D])
        xf = sb("xf", [P, NT, D])
        logits = sb("logits", [P, N])
        probs = sb("probs", [P, 2, N])
        probs_t = sb("probs_t", [P, NT, 2 * P])
        q_ab = sb("q_ab", [P, N], BF16)
        q_ac = sb("q_ac", [P, N], BF16)
        k_ab = sb("k_ab", [P, N], BF16)
        k_ba = sb("k_ba", [P, N], BF16)
        k_ca = sb("k_ca", [P, N], BF16)
        adj_buf = sb("adj_buf", [P, AB, JC, 2 * P])
        row_acc = sb("row_acc", [P, 4, 2 * P])
        x_pair = sb("x_pair", [P, 2, D])
        att_t = sb("att_t", [P, 2 * P])
        adj_out_t = sb("adj_out_t", [P, 2 * P])
        fin = sb("fin", [P, 2, 2, 2 * D])
        z_base = sb("z_base", [P, 2, D])
        z_pair = sb("z_pair", [P, 2, D])
        eye_sb = sb("eye_sb", [P, P])
        ones = sb("ones", [P, 1])
        zeros = sb("zeros", [P, 2 * P])
        w1_sb = sb("w1_sb", [DA, D])
        w2t_sb = sb("w2t_sb", [DA, DA])
        wq2 = sb("wq2", [D, 2, DA])
        wk2 = sb("wk2", [D, 2, DA])
        u_eye = sb("u_eye", [D, STEPS, 2, 2 * D])
        gain = sb("gain", [P, D])
        shift = sb("shift", [P, D])
        row_inv = sb("row_inv", [P, NT])
        kept_inv = sb("kept_inv", [P, NT])
        chunk_max = sb("chunk_max", [P, NC])
        neg_max = sb("neg_max", [P, 2])
        total = sb("total", [P, 2])
        stat = sb("stat", [P, 6, NT])
        s = sb("s", [P, 16])
        sb_junk = sb("junk", [P, N], BF16)
        x_t = probs_t[:, 0:2, :].rearrange("p a b -> p (a b)")
        part = [[probs_t[:, 4 + 4 * w + m, :].bitcast(BF16) for m in range(3)] for w in range(2)]
        rest = [probs_t[:, 12 + 2 * w:14 + 2 * w, :].rearrange("p a b -> p (a b)") for w in range(2)]

        loaded_x = sem("loaded_x")
        loaded_w = sem("loaded_w")
        normed = sem("normed")
        squared = sem("squared")
        consts = sem("consts")
        wq_ready = sem("wq_ready")
        w_ready = sem("w_ready")
        xt_ready = sem("xt_ready")
        xt_copied = sem("xt_copied")
        qk_ready = sem("qk_ready")
        part1_ready = sem("part1_ready")
        part1_sub = sem("part1_sub")
        qk_split = sem("qk_split")
        logits_ready = sem("logits_ready")
        logits_taken = sem("logits_taken")
        max_ready = sem("max_ready")
        exp_ready = sem("exp_ready")
        masked = sem("masked")
        turn_full = sem("turn_full")
        turn_free = sem("turn_free")
        att_done = sem("att_done")
        att_copied = sem("att_copied")
        adj_done = sem("adj_done")
        adj_copied = sem("adj_copied")
        adj_loaded = [sem(f"adj_loaded{c}") for c in range(AB)]
        adj_used = sem("adj_used")
        adj_summed = sem("adj_summed")
        rows_done = sem("rows_done")
        row_inv_ready = sem("row_inv_ready")
        x_pair_ready = sem("x_pair_ready")
        fin_ready = sem("fin_ready")
        z_ready = sem("z_ready")
        z_base_loaded = sem("z_base_loaded")
        stored = sem("stored")
        step_loaded = sem("step_loaded")
        step_done = sem("step_done")
        dve_seq = sem("dve_seq")
        pool_seq = sem("pool_seq")
        final_loaded = sem("final_loaded")
        final_stat = sem("final_stat")
        final_ready = sem("final_ready")
        out_stored = sem("out_stored")

        block = ctx.enter_context(nc.Block())

        def fill_base(step, p):
            return FILLS * step + NB + (p - 1) * (2 * NB + 2)

        def pairs(eng, body):
            body(0)
            with eng.Fori(1, PAIRS - 1) as p:
                body(p)
            body(PAIRS - 1)

        def is_first(p):
            return isinstance(p, int) and p == 0

        def is_last(p):
            return isinstance(p, int) and p == PAIRS - 1

        STORES = 3

        def stored_before(step, p):
            return 16 * (STORES * p if step == 0 else STORES * PAIRS + p)

        @block.sync
        def _(sp):
            sp.dma_start(xa[:], tiled(x)).then_inc(loaded_x, 16)
            sp.dma_start(eye_sb[:], eye).then_inc(loaded_w, 16)
            sp.dma_start(w1_sb[:], w1).then_inc(loaded_w, 16)
            sp.dma_start(w2t_sb[:], w2_t).then_inc(loaded_w, 16)
            for half in range(2):
                sp.dma_start(wk2[:, half, :], w3_t).then_inc(loaded_w, 16)
            for step in range(STEPS):
                sp.dma_start(u_eye[:, step, 0, 0:D], u2_t[step]).then_inc(loaded_w, 16)
                sp.dma_start(u_eye[:, step, 1, 0:D], u1_t[step]).then_inc(loaded_w, 16)
                for b in range(2):
                    sp.dma_start(u_eye[:, step, b, D:2 * D], eye).then_inc(loaded_w, 16)
            sp.dma_start(gain[:], ln_g.unsqueeze(0).to_broadcast([P, D])).then_inc(loaded_w, 16)
            sp.dma_start(shift[:], ln_b.unsqueeze(0).to_broadcast([P, D])).then_inc(loaded_w, 16)

            def load_adj(step, p, chunks=range(AC)):
                sp.to_reg(p * (2 * P) * 4)
                n = AC * (PAIRS * step + p)
                for c in chunks:
                    src = adj_t[c * JC * P:(c + 1) * JC * P, bass.ts(p, 2 * P)].rearrange("(j q) i -> q j i", q=P)
                    if not (step == 0 and is_first(p) and c < AB):
                        sp.wait_ge(adj_used, n - AB + c + 1)
                        if step == 0:
                            sp.wait_ge(adj_summed, n - AB + c + 1)
                        elif is_first(p):
                            sp.wait_ge(adj_summed, AC * PAIRS)
                    sp.dma_start(adj_buf[:, c % AB], src).then_inc(adj_loaded[c % AB], 16)

            def rows(ap, p):
                return tiled(ap)[:, bass.ts(p, 2), :]

            def store(step, p):
                sp.to_reg(p * 2 * P * D * 4)
                sp.wait_ge(z_ready, PAIRS * step + p + 1)
                sp.dma_start(rows(z_dram, p), z_pair[:]).then_inc(stored, 16)
                if step == 0:
                    sp.dma_start(rows(xa_dram, p), fin[:, 0, :, D:2 * D]).then_inc(stored, 16)
                    sp.dma_start(rows(xf_dram, p), fin[:, 1, :, D:2 * D]).then_inc(stored, 16)

            def load_base(p):
                sp.to_reg(p * 2 * P * D * 4)
                if not is_first(p):
                    sp.wait_ge(z_ready, PAIRS + p)
                sp.dma_start(z_base[:], rows(z_dram, p)).then_inc(z_base_loaded, 16)

            for step in range(STEPS):
                def body(p):
                    if step == 1 and not is_first(p):
                        load_base(p - 1)
                    if not is_last(p):
                        load_adj(step, p + 1)
                    if not is_first(p):
                        store(step, p - 1)

                if step == 0:
                    load_adj(0, 0)
                pairs(sp, body)
                if step == 1:
                    load_base(PAIRS - 1)
                else:
                    load_adj(1, 0, range(AB))
                store(step, PAIRS - 1)
                sp.wait_ge(stored, stored_before(1, 0) if step == 0 else stored_before(1, PAIRS))
                if step == 0:
                    sp.wait_ge(step_done, 2)
                    sp.dma_start(xa[:], tiled(xa_dram)).then_inc(step_loaded, 16)
                    sp.dma_start(xf[:], tiled(xf_dram)).then_inc(step_loaded, 16)
                    load_adj(1, 0, range(AB, AC))
            sp.wait_ge(step_done, 4)
            sp.dma_start(xa[:], tiled(z_dram)).then_inc(final_loaded, 16)
            sp.dma_start(xf[:], tiled(x)).then_inc(final_loaded, 16)
            sp.wait_ge(final_ready, 1)
            sp.dma_start(tiled(out), xf[:]).then_inc(out_stored, 16)
            sp.wait_ge(out_stored, 16)

        @block.tensor
        def _(pe):
            pe.wait_ge(loaded_w, 16 * (7 + 4 * STEPS - 0))
            for half in range(2):
                mm = pe.matmul(ps_att[:, half * DA:(half + 1) * DA], w1_sb[:], w2t_sb[:], start=True, stop=True)
            mm.then_inc(wq_ready, 1)

            def build_qk(step):
                for g in range(NB):
                    n = NB * step + g
                    if step == 0 and g == 0:
                        pe.wait_ge(normed, 1)
                        pe.wait_ge(w_ready, 1)
                    if step == 1 and g == 0:
                        pe.wait_ge(step_loaded, 32)
                        pe.wait_ge(turn_free, FILLS)
                    if n >= 2:
                        pe.wait_ge(xt_copied, n - 1)
                    for j in range(BANK // P):
                        mm = pe.transpose(ps_turn[:, g % 2, j * P:(j + 1) * P], xa[:, 4 * g + j, :], eye_sb[:])
                    mm.then_inc(xt_ready, 1)
                    pe.wait_ge(xt_copied, n + 1)
                    if n >= 1:
                        pe.wait_ge(qk_split, n)
                    pe.matmul(ps_logits[:, 0, 0:BANK], wq2[:].rearrange("p a b -> p (a b)"), x_t, start=True, stop=True)
                    pe.matmul(ps_logits[:, 1, 0:BANK], wk2[:].rearrange("p a b -> p (a b)"), x_t, start=True,
                              stop=True).then_inc(qk_ready, 1)

            def logits_of(step, t):
                for c in range(NC):
                    n = NC * NT * step + NC * t + c
                    if not (isinstance(n, int) and n < 2):
                        pe.wait_ge(logits_taken, n - 1)
                    for b in range(2):
                        dst = ps_logits[:, c % 2, b * BANK:(b + 1) * BANK]
                        cols = slice((2 * c + b) * BANK, (2 * c + b + 1) * BANK)
                        for m, (q, k) in enumerate(((q_ab, k_ab), (q_ab, k_ba), (q_ac, k_ca))):
                            mm = pe.matmul(dst, q[:, bass.ts(t, P)], k[:, cols], start=(m == 0), stop=(m == 2))
                    mm.then_inc(logits_ready, 1)

            def turn(step, t, par, base):
                pe.wait_ge(masked, NT * step + t + 1)
                for f in range(NB):
                    if not (isinstance(base, int) and base + f < 2):
                        pe.wait_ge(turn_free, base + f - 1)
                    for j in range(BANK // P):
                        blk = BANK // P * f + j
                        mm = pe.transpose(ps_turn[:, f % 2, j * P:(j + 1) * P], probs[:, par, blk * P:(blk + 1) * P],
                                          eye_sb[:])
                    mm.then_inc(turn_full, 1)

            def att_product(step, p, turned):
                pe.wait_ge(turn_free, turned)
                if not (isinstance(p, int) and step == 0 and p == 0):
                    pe.wait_ge(att_copied, PAIRS * step + p)
                    if step == 0:
                        pe.wait_ge(row_inv_ready, p)
                    elif is_first(p):
                        pe.wait_ge(row_inv_ready, PAIRS)
                for j in range(NT):
                    mm = pe.matmul(ps_att[:, 0:2 * P], xa[:, j, :], probs_t[:, j, :], start=(j == 0), stop=(j == NT - 1))
                mm.then_inc(att_done, 1)

            def adj_product(step, p, chunks):
                n = PAIRS * step + p
                for c in chunks:
                    if c == 0 and not (isinstance(n, int) and n == 0):
                        pe.wait_ge(adj_copied, n)
                    pe.wait_ge(adj_loaded[c % AB], (n * (AC // AB) + c // AB + 1) * 16)
                    for j in range(JC):
                        mm = pe.matmul(ps_adj[:, 0:2 * P], xf[:, JC * c + j, :], adj_buf[:, c % AB, j, :],
                                       start=(c == 0 and j == 0), stop=False, skip_group_check=True)
                    mm.then_inc(adj_used, 1)
                if chunks[-1] == AC - 1:
                    pe.wait_ge(x_pair_ready, n + 1)
                    for tile in range(2):
                        mm = pe.matmul(ps_adj[:, tile * P:(tile + 1) * P], x_pair[:, tile, :], eye_sb[:], start=False,
                                       stop=(tile == 1), skip_group_check=True)
                    mm.then_inc(adj_done, 1)

            def finish(step, p, base):
                n = PAIRS * step + p
                width = 2 * D if step == 0 else D
                for b, (src, ready) in enumerate(((att_t, att_copied), (adj_out_t, adj_copied))):
                    pe.wait_ge(ready, n + 1)
                    pe.wait_ge(turn_free, base + b - 1)
                    for tile in range(2):
                        mm = pe.matmul(ps_turn[:, b, tile * 2 * D:tile * 2 * D + width], src[:, tile * P:(tile + 1) * P],
                                       u_eye[:, step, b, 0:width], start=True, stop=True)
                    mm.then_inc(turn_full, 1)
                if step == 0:
                    pe.wait_ge(adj_summed, (p + 1) * AC)
                    for tile in range(2):
                        for m in range(4):
                            mm = pe.matmul(ps_att[:, tile:tile + 1], row_acc[:, m, tile * P:(tile + 1) * P], ones[:],
                                           start=(m == 0), stop=(m == 3))
                    mm.then_inc(rows_done, 1)

            for step in range(STEPS):
                build_qk(step)
                pe.wait_ge(qk_split, NB * (step + 1))
                logits_of(step, 0)

                def body(p):
                    logits_of(step, 2 * p + 1)
                    if not is_first(p):
                        base = fill_base(step, p)
                        turn(step, 2 * p - 1, 1, base)
                        att_product(step, p - 1, base + NB)
                    adj_product(step, p, range(0, AC // 2))
                    if not is_first(p):
                        finish(step, p - 1, base + NB)
                    if not is_last(p):
                        logits_of(step, 2 * p + 2)
                    turn(step, 2 * p, 0, FILLS * step if is_first(p) else base + NB + 2)
                    adj_product(step, p, range(AC // 2, AC))

                pairs(pe, body)
                base = fill_base(step, PAIRS)
                turn(step, NT - 1, 1, base)
                att_product(step, PAIRS - 1, base + NB)
                finish(step, PAIRS - 1, base + NB)
                pe.drain().then_inc(step_done, 1)

        @block.scalar
        def _(act):
            act.wait_ge(squared, 1)
            act.activation(logits[:], xa[:].rearrange("p t d -> p (t d)"), ACT.Square).then_inc(squared, 1)
            act.wait_ge(squared, 3)
            act.activation(stat[:, 3, :], stat[:, 2, :], ACT.Sqrt).then_inc(squared, 1)
            act.wait_ge(wq_ready, 1)
            act.activation(wq2[:].rearrange("p a b -> p (a b)"), ps_att[:, 0:2 * DA], ACT.Copy).then_inc(w_ready, 1)

            def build_qk(step):
                for g in range(NB):
                    n = NB * step + g
                    act.wait_ge(xt_ready, n + 1)
                    if n >= 1:
                        act.wait_ge(qk_ready, n)
                    act.activation(x_t, ps_turn[:, g % 2, :], ACT.Copy).then_inc(xt_copied, 1)
                    act.wait_ge(qk_ready, n + 1)
                    if n >= 1:
                        act.wait_ge(qk_split, n)
                    for w in range(2):
                        act.activation(part[w][0], ps_logits[:, w, 0:BANK], ACT.Copy).then_inc(part1_ready, 1)
                    for w in range(2):
                        act.wait_ge(part1_sub, 2 * n + w + 1)
                        act.activation(part[w][1], rest[w], ACT.Copy).then_inc(part1_ready, 1)

            def exp_of(step, t, par):
                n = NT * step + t
                act.wait_ge(max_ready, n + 1)
                act.activation(probs[:, par, :], logits[:], ACT.Exp, bias=neg_max[:, par:par + 1],
                               accum_out=total[:, par:par + 1]).then_inc(exp_ready, 1)

            def take_turned(base, par):
                for f in range(NB):
                    act.wait_ge(turn_full, base + f + 1)
                    act.activation(probs_t[:, 4 * f:4 * f + 4, par * P:(par + 1) * P],
                                   ps_turn[:, f % 2, :].rearrange("p (j i) -> p j i", i=P),
                                   ACT.Copy).then_inc(turn_free, 1)

            def copy_adj(step, p):
                n = PAIRS * step + p
                act.wait_ge(adj_done, n + 1)
                if not (isinstance(n, int) and n == 0):
                    act.wait_ge(turn_full, fill_of_finish(step, p - 1))
                act.activation(adj_out_t[:], ps_adj[:, 0:2 * P], ACT.Copy).then_inc(adj_copied, 1)

            def fill_of_finish(step, p):
                if isinstance(p, int) and p < 0:
                    return FILLS * step
                return fill_base(step, p + 1) + NB + 2

            def copy_att(step, p):
                n = PAIRS * step + p
                act.wait_ge(att_done, n + 1)
                act.activation(att_t[:], ps_att[:, 0:2 * P], ACT.Copy).then_inc(att_copied, 1)

            def take_finished(step, p, base, b):
                width = 2 * D if step == 0 else D
                act.wait_ge(turn_full, base + b + 1)
                if b == 0:
                    act.wait_ge(masked, NT * step + 2 * p + 2)
                    if not (step == 0 and isinstance(p, int) and p == 0):
                        act.wait_ge(stored, stored_before(step, p))
                        act.wait_ge(z_ready, PAIRS * step + p)
                elif step == 0:
                    act.wait_ge(row_inv_ready, p + 1)
                inv = kept_inv if b == 0 else row_inv
                for tile in range(2):
                    last = act.activation(fin[:, b, tile, 0:width], ps_turn[:, b, tile * 2 * D:tile * 2 * D + width],
                                          ACT.Copy, scale=inv[:, bass.ds(2 * p + tile, 1)])
                    last.then_inc(fin_ready, 1)
                act.drain().then_inc(turn_free, 1)

            for step in range(STEPS):
                build_qk(step)
                act.wait_ge(qk_split, NB * (step + 1))
                exp_of(step, 0, 0)

                def body(p):
                    if not is_first(p):
                        base = fill_base(step, p)
                        copy_adj(step, p - 1)
                        take_turned(base, 1)
                    exp_of(step, 2 * p + 1, 1)
                    if not is_first(p):
                        copy_att(step, p - 1)
                        take_finished(step, p - 1, base + NB, 0)
                        take_finished(step, p - 1, base + NB, 1)
                    take_turned(FILLS * step if is_first(p) else base + NB + 2, 0)
                    if not is_last(p):
                        exp_of(step, 2 * p + 2, 0)

                pairs(act, body)
                base = fill_base(step, PAIRS)
                copy_adj(step, PAIRS - 1)
                take_turned(base, 1)
                copy_att(step, PAIRS - 1)
                take_finished(step, PAIRS - 1, base + NB, 0)
                take_finished(step, PAIRS - 1, base + NB, 1)
            act.wait_ge(final_stat, 1)
            act.activation(logits[:], xa[:].rearrange("p t d -> p (t d)"), ACT.Square).then_inc(final_stat, 1)
            act.wait_ge(final_stat, 3)
            act.activation(stat[:, 3, :], stat[:, 2, :], ACT.Sqrt).then_inc(final_stat, 1)

        @block.gpsimd
        def _(pool):
            pool.memset(ones[:], 1.0).then_inc(consts, 1)
            pool.memset(zeros[:], 0.0).then_inc(consts, 1)
            pool.wait_ge(consts, 2)
            no_x = zeros[:, 0:D].unsqueeze(1).to_broadcast([P, 2, D])
            no_row = zeros[:].unsqueeze(1).to_broadcast([P, JC, 2 * P])

            def sum_rows(p):
                if not is_first(p):
                    pool.wait_ge(rows_done, p)
                for c in range(AC):
                    pool.wait_ge(adj_loaded[c % AB], (p * (AC // AB) + c // AB + 1) * 16)
                    if c == 0:
                        pool.tensor_tensor(row_acc[:], adj_buf[:, c], no_row, ALU.add).then_inc(adj_summed, 1)
                    else:
                        pool.wait_ge(adj_summed, p * AC + c)
                        pool.tensor_tensor(row_acc[:], row_acc[:], adj_buf[:, c % AB], ALU.add)\
                            .then_inc(adj_summed, 1)

            def add_z(step, p):
                n = PAIRS * step + p
                pool.wait_ge(fin_ready, 4 * (n + 1))
                if not (step == 0 and isinstance(p, int) and p == 0):
                    pool.wait_ge(stored, stored_before(step, p))
                pool.tensor_tensor(z_pair[:], fin[:, 0, :, 0:D], fin[:, 1, :, 0:D], ALU.add).then_inc(pool_seq, 1)
                pool.wait_ge(pool_seq, 1)
                if step == 0:
                    pool.tensor_tensor(z_pair[:], z_pair[:], xa[:, bass.ts(p, 2), :], ALU.add).then_inc(z_ready, 1)
                else:
                    pool.wait_ge(z_base_loaded, (p + 1) * 16)
                    pool.tensor_tensor(z_pair[:], z_pair[:], z_base[:], ALU.add).then_inc(z_ready, 1)
                pool.sem_clear(pool_seq)

            for step in range(STEPS):
                if step == 0:
                    pool.wait_ge(normed, 2)
                else:
                    pool.wait_ge(step_loaded, 32)

                def body(p):
                    n = PAIRS * step + p
                    if not (isinstance(n, int) and n == 0):
                        pool.wait_ge(adj_done, n)
                    rows_in = xf[:, bass.ts(p, 2), :]
                    pool.tensor_tensor(x_pair[:], rows_in, no_x, ALU.add).then_inc(x_pair_ready, 1)
                    if step == 0:
                        sum_rows(p)
                    if not is_first(p):
                        add_z(step, p - 1)

                pairs(pool, body)
                add_z(step, PAIRS - 1)
                pool.wait_ge(z_ready, PAIRS * (step + 1))
                pool.sem_inc(step_done, 1)

        @block.vector
        def _(dve):
            chain = [0]

            def link(ins):
                chain[0] += 1
                ins.then_inc(dve_seq, 1)
                dve.wait_ge(dve_seq, chain[0])

            def restart():
                dve.sem_clear(dve_seq)
                chain[0] = 0

            def spread(v):
                return v.unsqueeze(2).to_broadcast([P, NT, D])

            dve.wait_ge(loaded_x, 16)
            link(dve.tensor_reduce(stat[:, 0, :], xa[:], AX.X, ALU.add))
            link(dve.tensor_scalar(stat[:, 1, :], stat[:, 0, :], 1.0 / D, None, ALU.mult))
            dve.tensor_tensor(xa[:], xa[:], spread(stat[:, 1, :]), ALU.subtract).then_inc(squared, 1)
            dve.wait_ge(squared, 2)
            link(dve.tensor_reduce(stat[:, 0, :], logits[:].rearrange("p (t d) -> p t d", d=D), AX.X, ALU.add))
            dve.tensor_scalar(stat[:, 2, :], stat[:, 0, :], 1.0 / D, LN_EPS, ALU.mult, ALU.add).then_inc(squared, 1)
            dve.wait_ge(squared, 4)
            link(dve.reciprocal(stat[:, 4, :], stat[:, 3, :]))
            link(dve.tensor_tensor(xa[:], xa[:], spread(stat[:, 4, :]), ALU.mult))
            link(dve.tensor_scalar(xa[:], xa[:], 0.0, None, ALU.max))
            dve.tensor_copy(xf[:], xa[:]).then_inc(normed, 1)
            dve.wait_ge(normed, 1)
            dve.sem_inc(normed, 1)

            def build_qk(step):
                lo, hi = slice(0, DA), slice(DA, 2 * DA)
                for g in range(NB):
                    n = NB * step + g
                    cols = slice(g * BANK, (g + 1) * BANK)
                    for w in range(2):
                        dve.wait_ge(part1_ready, 4 * n + w + 1)
                        dve.tensor_tensor(rest[w], ps_logits[:, w, 0:BANK], part[w][0], ALU.subtract)\
                            .then_inc(part1_sub, 1)
                    for w, places in enumerate((((q_ab, 0, 1), (q_ac, 0, 2)),
                                                ((k_ab, 0, 1), (k_ba, 1, 0), (k_ca, 2, 0)))):
                        dve.wait_ge(part1_ready, 4 * n + 2 + w + 1)
                        link(dve.tensor_tensor(part[w][2], rest[w], part[w][1], ALU.subtract))
                        for dst, a, b in places:
                            dve.tensor_copy(dst[lo, cols], part[w][a][lo, :])
                            last = dve.tensor_copy(dst[hi, cols], part[w][b][hi, :])
                            if not (w == 1 and dst is k_ca):
                                link(last)
                            else:
                                last.then_inc(qk_split, 1)

            def take_logits(step, t, par):
                for c in range(NC):
                    n = NC * NT * step + NC * t + c
                    dve.wait_ge(logits_ready, n + 1)
                    if c == 0 and not (isinstance(n, int) and n == 0):
                        dve.wait_ge(exp_ready, NT * step + t)
                    dve.tensor_scalar(logits[:, c * CHUNK:(c + 1) * CHUNK], ps_logits[:, c % 2, :], 1.0, None,
                                      ALU.mult, ALU.max, accum_out=chunk_max[:, c:c + 1]).then_inc(logits_taken, 1)
                dve.wait_ge(logits_taken, NC * NT * step + NC * t + NC)
                dve.tensor_reduce(neg_max[:, par:par + 1], chunk_max[:], AX.X, ALU.max, negate=True)\
                    .then_inc(max_ready, 1)

            goal, low, high, mid, mass, up, gate = (s[:, i:i + 1] for i in range(7))

            def search(step, t, par):
                e = probs[:, par, :]
                restart()
                dve.wait_ge(exp_ready, NT * step + t + 1)
                link(dve.tensor_scalar(goal, total[:, par:par + 1], TOP_P, None, ALU.mult))
                link(dve.memset(low, 0.0))
                link(dve.memset(high, 2.0))
                with dve.Fori(0, BISECTIONS) as _i:
                    restart()
                    link(dve.tensor_scalar(mid, low, high, 0.5, ALU.add, ALU.mult))
                    link(dve.scalar_tensor_tensor(out=junk, in0=e, scalar=mid, in1=e, op0=ALU.is_gt, op1=ALU.mult,
                                                  accum_out=mass))
                    link(dve.tensor_scalar(up, mass, goal, mid, ALU.is_ge, ALU.mult))
                    link(dve.tensor_scalar(gate, mass, goal, 4.0, ALU.is_ge, ALU.mult))
                    link(dve.tensor_scalar(low, low, up, None, ALU.max))
                    link(dve.tensor_scalar(high, gate, mid, high, ALU.add, ALU.min))
                restart()
                link(dve.scalar_tensor_tensor(out=e, in0=e, scalar=low, in1=e, op0=ALU.is_gt, op1=ALU.mult,
                                              accum_out=mass))
                link(dve.tensor_scalar(up, mass, 1e-12, None, ALU.max))
                dve.reciprocal(kept_inv[:, bass.ds(t, 1)], up).then_inc(masked, 1)

            def invert_rows(p):
                restart()
                dve.wait_ge(rows_done, p + 1)
                link(dve.tensor_scalar(s[:, 8:10], ps_att[:, 0:2], 1.0, None, ALU.add))
                dve.reciprocal(row_inv[:, bass.ts(p, 2)], s[:, 8:10]).then_inc(row_inv_ready, 1)

            junk = sb_junk[:]
            for step in range(STEPS):
                build_qk(step)
                take_logits(step, 0, 0)

                def body(p):
                    take_logits(step, 2 * p + 1, 1)
                    search(step, 2 * p, 0)
                    if step == 0 and not is_first(p):
                        invert_rows(p - 1)
                    if not is_last(p):
                        take_logits(step, 2 * p + 2, 0)
                    search(step, 2 * p + 1, 1)

                pairs(dve, body)
                if step == 0:
                    invert_rows(PAIRS - 1)
            dve.wait_ge(final_loaded, 32)
            restart()
            link(dve.tensor_reduce(stat[:, 0, :], xa[:], AX.X, ALU.add))
            link(dve.tensor_scalar(stat[:, 1, :], stat[:, 0, :], 1.0 / D, None, ALU.mult))
            dve.tensor_tensor(xa[:], xa[:], spread(stat[:, 1, :]), ALU.subtract).then_inc(final_stat, 1)
            dve.wait_ge(final_stat, 2)
            link(dve.tensor_reduce(stat[:, 0, :], logits[:].rearrange("p (t d) -> p t d", d=D), AX.X, ALU.add))
            dve.tensor_scalar(stat[:, 2, :], stat[:, 0, :], 1.0 / D, LN_EPS, ALU.mult, ALU.add).then_inc(final_stat, 1)
            dve.wait_ge(final_stat, 4)
            link(dve.reciprocal(stat[:, 4, :], stat[:, 3, :]))
            link(dve.tensor_tensor(xa[:], xa[:], spread(stat[:, 4, :]), ALU.mult))
            link(dve.tensor_tensor(xa[:], xa[:], gain[:].unsqueeze(1).to_broadcast([P, NT, D]), ALU.mult))
            link(dve.tensor_tensor(xf[:], xf[:], shift[:].unsqueeze(1).to_broadcast([P, NT, D]), ALU.add))
            dve.tensor_tensor(xf[:], xf[:], xa[:], ALU.add).then_inc(final_ready, 1)


def kernel(x, adj, L0_gnn_W1, L0_gnn_W2, L0_gnn_W3, L0_gnn_U1, L0_gnn_U2, L0_gnn_ln_g, L0_gnn_ln_b):
    import numpy as np
    import concourse.bacc as bacc
    from concourse.bass_utils import run_bass_kernel_spmd as run

    nc = bacc.Bacc("TRN2", target_bir_lowering=False, num_devices=1)
    arrays = {
        "x": np.ascontiguousarray(x),
        "adj_t": np.ascontiguousarray(np.asarray(adj).T),
        "w1": np.ascontiguousarray(L0_gnn_W1),
        "w2_t": np.ascontiguousarray(np.asarray(L0_gnn_W2).T),
        "w3_t": np.ascontiguousarray(np.asarray(L0_gnn_W3).T),
        "u1_t": np.ascontiguousarray(np.asarray(L0_gnn_U1).transpose(0, 2, 1)),
        "u2_t": np.ascontiguousarray(np.asarray(L0_gnn_U2).transpose(0, 2, 1)),
        "ln_g": np.ascontiguousarray(L0_gnn_ln_g),
        "ln_b": np.ascontiguousarray(L0_gnn_ln_b),
        "eye": np.eye(P, dtype=np.float32),
    }
    args = [nc.dram_tensor(n, a.shape, F32, kind="ExternalInput").ap() for n, a in arrays.items()]
    out = nc.dram_tensor("out", arrays["x"].shape, F32, kind="ExternalOutput").ap()
    program(nc, *args, out)
    r = run(nc, [arrays], core_ids=[0])
    return r.results[0]["out"]
```
